# Optimizing a Trainium2 kernel written in Bass

```python
import numpy as np
import jax
import jax.numpy as jnp

def _softmax(x, axis=-1):
    return jax.nn.softmax(x, axis=axis)

def _gelu(x):
    return jax.nn.gelu(x, approximate=True)

def _silu(x):
    return jax.nn.silu(x)

def _sigmoid(x):
    return jax.nn.sigmoid(x)

def _layernorm(x, axis=-1, eps=1e-05):
    m = jnp.mean(x, axis=axis, keepdims=True)
    v = jnp.var(x, axis=axis, keepdims=True)
    return (x - m) / jnp.sqrt(v + eps)

def _scatter_add(tgt, idx, src, axis=0):
    return tgt.at[idx].add(src)

def _segment_sum(src, seg, n):
    return jax.ops.segment_sum(src, seg, n)
kernel_name = 'mk_adj_resnorm_d1_adj_r2_0abff3'

def setup_inputs(seed: int=0):
    np.random.seed(seed)
    _w = jnp.asarray

    def _rec_inputs():
        import jax
        import jax.numpy as jnp
        _gk = jax.random.key(seed)
        x = -0.001547 + 1.001 * jax.random.normal(jax.random.fold_in(_gk, 1), (512, 128), jnp.float32)
        _w = (1.0 + jnp.arange(512, dtype=jnp.float32)) ** (-0.5)
        _w = _w / _w.mean()
        _pij = jnp.clip(0.03125 * _w[:, None] * _w[None, :], 0.0, 1.0)
        _a = jax.random.uniform(jax.random.fold_in(_gk, 2), (512, 512)) < _pij
        adj = _a.astype(jnp.int32)
        return (x, adj)
    x, adj = _rec_inputs()

    def _L0_gnn_setup():
        import jax, jax.numpy as jnp
        import numpy as np
        BT, BN, D, H = (512, 512, 128, 8)
        DH = D // H
        key = jax.random.key(seed)
        ks = jax.random.split(key, 16)
        s = 1.0 / np.sqrt(D)
        return {'h_target': jax.random.normal(ks[0], (BT, D), jnp.float32), 'h_neigh': jax.random.normal(ks[1], (BN, D), jnp.float32), 'adjacency': jax.random.randint(ks[2], (BT, BN), 0, 2, jnp.int32), 'edge_types': jax.random.randint(ks[3], (BT, BN), 0, 2, jnp.int32), 'Wq': jax.random.normal(ks[4], (D, D), jnp.float32) * s, 'bq': jnp.zeros((D,), jnp.float32), 'Wk': jax.random.normal(ks[5], (D, D), jnp.float32) * s, 'bk': jnp.zeros((D,), jnp.float32), 'Wv': jax.random.normal(ks[6], (D, D), jnp.float32) * s, 'bv': jnp.zeros((D,), jnp.float32), 'Wo': jax.random.normal(ks[7], (D, D), jnp.float32) * s, 'bo': jnp.zeros((D,), jnp.float32), 'E': jax.random.normal(ks[8], (2, D), jnp.float32)}
    _L0_gnn_all = _L0_gnn_setup()
    _L0_gnn_in = {k: v for k, v in _L0_gnn_all.items() if k in ('h_neigh', 'Wq', 'bq', 'Wk', 'bk', 'Wv', 'bv', 'Wo', 'bo', 'E')}
    del _L0_gnn_all
    return {'x': x, 'adj': adj, 'L0_gnn_h_neigh': _L0_gnn_in['h_neigh'], 'L0_gnn_Wq': _L0_gnn_in['Wq'], 'L0_gnn_bq': _L0_gnn_in['bq'], 'L0_gnn_Wk': _L0_gnn_in['Wk'], 'L0_gnn_bk': _L0_gnn_in['bk'], 'L0_gnn_Wv': _L0_gnn_in['Wv'], 'L0_gnn_bv': _L0_gnn_in['bv'], 'L0_gnn_Wo': _L0_gnn_in['Wo'], 'L0_gnn_bo': _L0_gnn_in['bo'], 'L0_gnn_E': _L0_gnn_in['E']}

def reference(x, adj, L0_gnn_h_neigh, L0_gnn_Wq, L0_gnn_bq, L0_gnn_Wk, L0_gnn_bk, L0_gnn_Wv, L0_gnn_bv, L0_gnn_Wo, L0_gnn_bo, L0_gnn_E):
    import jax
    import jax.numpy as jnp

    def _L0_gnn_ref(h_target, h_neigh, adjacency, edge_types, Wq, bq, Wk, bk, Wv, bv, Wo, bo, E):
        import jax, jax.numpy as jnp
        import numpy as np
        BT, BN, D, H = (512, 512, 128, 8)
        DH = D // H
        Bt, d = h_target.shape
        Bn = h_neigh.shape[0]
        msg = h_neigh[None, :, :] + E[edge_types]
        q = (h_target @ Wq.T + bq).reshape(Bt, H, DH)
        k = (msg @ Wk.T + bk).reshape(Bt, Bn, H, DH)
        v = (msg @ Wv.T + bv).reshape(Bt, Bn, H, DH)
        scores = jnp.einsum('bhd,bnhd->bhn', q, k) / np.sqrt(DH).astype(np.float32)
        mask = adjacency[:, None, :] == 0
        scores = jnp.where(mask, jnp.float32(-1000000000.0), scores)
        attn = jax.nn.softmax(scores, axis=-1)
        attn = jnp.where(mask, jnp.float32(0.0), attn)
        out = jnp.einsum('bhn,bnhd->bhd', attn, v).reshape(Bt, d)
        return out @ Wo.T + bo
    x = _layernorm(x + _L0_gnn_ref(x, L0_gnn_h_neigh, adj, adj, L0_gnn_Wq, L0_gnn_bq, L0_gnn_Wk, L0_gnn_bk, L0_gnn_Wv, L0_gnn_bv, L0_gnn_Wo, L0_gnn_bo, L0_gnn_E), axis=-1)
    return x

_drawn_inputs = setup_inputs


def setup_inputs(seed=0):
    import zlib

    import numpy as np

    out = dict(_drawn_inputs(seed))
    spreads = {'L0_gnn_bq': (0.0, 0.435),
     'L0_gnn_bk': (0.0, 0.8),
     'L0_gnn_bv': (0.0, 0.1),
     'L0_gnn_bo': (0.0, 0.1)}
    factors = {}
    for name, (base, spread) in spreads.items():
        noise = np.random.default_rng([zlib.crc32(name.encode()), seed]).standard_normal(out[name].shape)
        drawn = base * np.exp(spread * noise) if base else spread * noise
        out[name] = jnp.asarray(drawn.astype(out[name].dtype))
    for name, factor in factors.items():
        out[name] = (out[name] * factor).astype(out[name].dtype)
    return out
```

```python
import concourse.bass as bass
from concourse import mybir
from contextlib import ExitStack

PARTS = 128
N_HEADS = 8
D_MODEL = 128
D_HEAD = D_MODEL // N_HEADS
N_TARGETS = 512
N_NEIGHBOURS = 512
TILES = N_TARGETS // PARTS
CHUNKS = N_NEIGHBOURS // PARTS
GROUP = 4
N_GROUPS = N_HEADS // GROUP
LANE = PARTS // GROUP
QUERY_PARTS = (0, 0, 0, 1, 1, 2)
KEY_PARTS = (0, 1, 2, 0, 1, 0)
SCORE_ROWS = len(QUERY_PARTS) * D_HEAD
SHIFTED_ROWS = SCORE_ROWS + 2
MASK_BIAS = -float(2 ** 30)
MAX_FLOOR = -float(2 ** 29)
SCORE_SCALE = float(D_HEAD) ** -0.5
TINY = 1e-30
EPS = 1e-5
LEAD = 6


def graph_attention(
    nc: bass.Bass,
    q_pack: bass.AP,
    k_pack: bass.AP,
    v_pack: bass.AP,
    x: bass.AP,
    adj: bass.AP,
    adj_t: bass.AP,
    bv: bass.AP,
    bo: bass.AP,
    out: bass.AP,
):
    fp32 = mybir.dt.float32
    bf16 = mybir.dt.bfloat16
    i32 = mybir.dt.int32
    ALU = mybir.AluOpType
    ACT = mybir.ActivationFunctionType
    T, N, D = N_TARGETS, N_NEIGHBOURS, D_MODEL

    with ExitStack() as ctx:
        def sb(name, shape, dt):
            return ctx.enter_context(nc.sbuf_tensor(name, shape, dt))

        def pb(name, shape):
            return ctx.enter_context(nc.psum_tensor(name, shape, fp32))

        def sem(name):
            return ctx.enter_context(nc.semaphore(name))

        q_in = sb("q_in", [PARTS, T + D + 1], fp32)
        k_in = sb("k_in", [PARTS, N + D + 3], fp32)
        v_in = sb("v_in", [PARTS, D * 5], fp32)
        x_t, wq_t, bq_col = q_in[:, 0:T], q_in[:, T:T + D], q_in[:, T + D:T + D + 1]
        h_t, wk_t, bk_col = k_in[:, 0:N], k_in[:, N:N + D], k_in[:, N + D:N + D + 1]
        edge_col = k_in[:, N + D + 2:N + D + 3]
        wv_t = v_in[:, 0:D]
        wo_pad = v_in[:, D:3 * D].rearrange("p (g n) -> p g n", g=N_GROUPS)
        sum_selector = v_in[:, 3 * D:4 * D]
        identity = v_in[:, 4 * D:5 * D]
        x_rows = sb("x_rows", [PARTS, TILES, D], fp32)
        adj_rows = sb("adj_rows", [PARTS, TILES, N], i32)
        adj_cols = sb("adj_cols", [PARTS, CHUNKS, T], i32)
        bv_all = sb("bv_all", [PARTS, D], fp32)
        bo_all = sb("bo_all", [PARTS, D], fp32)
        identity_b = sb("identity_b", [PARTS, PARTS], bf16)
        bias_rows = sb("bias_rows", [PARTS, TILES, N], bf16)
        bias_cols = sb("bias_cols", [PARTS, CHUNKS, T], bf16)
        msg_t = sb("msg_t", [PARTS, N], fp32)
        q_full = sb("q_full", [PARTS, T], fp32)
        k_full = sb("k_full", [PARTS, N], fp32)
        q_rest = sb("q_rest", [PARTS, T], fp32)
        k_rest = sb("k_rest", [PARTS, N], fp32)
        q_part = sb("q_part", [PARTS, 3, T], bf16)
        k_part = sb("k_part", [PARTS, 3, N], bf16)
        queries = sb("queries", [PARTS, N_HEADS, T], bf16)
        keys = sb("keys", [PARTS, N_HEADS, N], bf16)
        values = sb("values", [PARTS, CHUNKS, N_HEADS, LANE], fp32)
        masked = sb("masked", [PARTS, 4, N], bf16)
        row_max = sb("row_max", [PARTS, N_HEADS, TILES], fp32)
        neg_max = sb("neg_max", [PARTS, N_HEADS, TILES, 2], bf16)
        probs = sb("probs", [PARTS, N_HEADS, CHUNKS, T], fp32)
        mixed = sb("mixed", [PARTS, N_GROUPS, T], fp32)
        total = sb("total", [PARTS, N_GROUPS, T], fp32)
        per_total = sb("per_total", [PARTS, N_GROUPS, T], fp32)
        mixed_n = sb("mixed_n", [PARTS, N_GROUPS, T], fp32)
        resid = sb("resid", [PARTS, TILES, D], fp32)
        resid_0 = sb("resid_0", [PARTS, TILES, D], fp32)
        y = sb("y", [PARTS, TILES, D], fp32)
        stats = sb("stats", [PARTS, TILES, 6], fp32)
        moments = sb("moments", [PARTS, TILES, 2], fp32)
        variance = sb("variance", [PARTS, TILES], fp32)
        deviation = sb("deviation", [PARTS, TILES], fp32)
        rstd = sb("rstd", [PARTS, TILES], fp32)
        normed = sb("normed", [PARTS, TILES, D], fp32)

        col_ps = pb("col_ps", [PARTS, 2, 2, T])
        row_ps = pb("row_ps", [PARTS, 2, N])
        mix_ps = pb("mix_ps", [PARTS, T])
        misc_ps = pb("misc_ps", [PARTS, T])

        q_loaded = sem("q_loaded")
        k_loaded = sem("k_loaded")
        v_loaded = sem("v_loaded")
        adj_rows_loaded = sem("adj_rows_loaded")
        adj_cols_loaded = sem("adj_cols_loaded")
        bv_loaded = sem("bv_loaded")
        resid_loaded = sem("resid_loaded")
        msg_ready = sem("msg_ready")
        q_projected = sem("q_projected")
        k_projected = sem("k_projected")
        v_projected = sem("v_projected")
        q_full_ready = sem("q_full_ready")
        k_full_ready = sem("k_full_ready")
        q_rest_ready = sem("q_rest_ready")
        k_rest_ready = sem("k_rest_ready")
        q_part_ready = [sem(f"q_part{n}_ready") for n in range(3)]
        k_part_ready = [sem(f"k_part{n}_ready") for n in range(3)]
        stacked = sem("stacked")
        ones_ready = sem("ones_ready")
        value_ones_ready = sem("value_ones_ready")
        values_ready = sem("values_ready")
        identity_ready = sem("identity_ready")
        bias_rows_ready = sem("bias_rows_ready")
        bias_cols_ready = sem("bias_cols_ready")
        rows_scored = sem("rows_scored")
        rows_maxed = sem("rows_maxed")
        neg_max_high = sem("neg_max_high")
        neg_max_ready = sem("neg_max_ready")
        max_turned = sem("max_turned")
        max_rows_ready = sem("max_rows_ready")
        cols_scored = sem("cols_scored")
        exps_done = sem("exps_done")
        mixed_done = sem("mixed_done")
        mixed_copied = sem("mixed_copied")
        totals_spread = sem("totals_spread")
        total_ready = sem("total_ready")
        per_total_ready = sem("per_total_ready")
        mixed_n_ready = sem("mixed_n_ready")
        resid_ready = sem("resid_ready")
        projected_out = sem("projected_out")
        resid_0_ready = sem("resid_0_ready")
        y_ready = sem("y_ready")
        stats_ready = sem("stats_ready")
        moments_ready = sem("moments_ready")
        variance_ready = sem("variance_ready")
        deviation_ready = sem("deviation_ready")
        rstd_ready = sem("rstd_ready")
        normed_ready = sem("normed_ready")
        stored = sem("stored")

        N_STACKS = 2 * len(QUERY_PARTS)

        def stack(eng, dst, part, block, n):
            rows = dst[D_HEAD * block:D_HEAD * (block + 1), :, :]
            eng.dma_start(rows, part[:, n, :]).then_inc(stacked, 16)

        block = ctx.enter_context(nc.Block())

        @block.sync
        def _(sp):
            sp.dma_start(q_in[:], q_pack).then_inc(q_loaded, 16)
            sp.dma_start(k_in[:], k_pack).then_inc(k_loaded, 16)
            sp.dma_start(adj_rows[:], adj.rearrange("(t p) n -> p t n", p=PARTS)).then_inc(adj_rows_loaded, 16)
            sp.dma_start(adj_cols[:], adj_t.rearrange("(c p) t -> p c t", p=PARTS)).then_inc(adj_cols_loaded, 16)
            sp.dma_start(x_rows[:], x.rearrange("(t p) d -> p t d", p=PARTS)).then_inc(resid_loaded, 16)
            sp.dma_start(bo_all[:], bo.to_broadcast([PARTS, D])).then_inc(resid_loaded, 16)
            for n in range(3):
                for ready, dst, part, where in ((q_part_ready, queries, q_part, QUERY_PARTS),
                                                (k_part_ready, keys, k_part, KEY_PARTS)):
                    sp.wait_ge(ready[n], 1)
                    for b, m in enumerate(where):
                        if m == n:
                            stack(sp, dst, part, b, n)
            for t in range(TILES):
                sp.wait_ge(normed_ready, t + 1)
                sp.dma_start(out[t * PARTS:(t + 1) * PARTS, :], normed[:, t, :]).then_inc(stored, 16)
            sp.wait_ge(stored, 16 * TILES)

        @block.gpsimd
        def _(pool):
            pool.dma_start(v_in[:], v_pack).then_inc(v_loaded, 16)
            pool.dma_start(bv_all[:], bv.to_broadcast([PARTS, D])).then_inc(bv_loaded, 16)
            nc.gpsimd.memset(keys[SCORE_ROWS:SHIFTED_ROWS, :, :], 1.0).then_inc(ones_ready, 1)
            pool.wait_ge(ones_ready, 1)
            nc.gpsimd.memset(values[:, :, :, D_HEAD:LANE], 1.0).then_inc(value_ones_ready, 1)
            pool.wait_ge(v_loaded, 16)
            pool.wait_ge(value_ones_ready, 1)
            nc.gpsimd.tensor_copy(identity_b[:], identity).then_inc(identity_ready, 1)
            pool.wait_ge(identity_ready, 1)
            pool.wait_ge(resid_loaded, 32)
            nc.gpsimd.tensor_tensor(resid[:], x_rows[:],
                                    bo_all[:].unsqueeze(1).to_broadcast([PARTS, TILES, D]),
                                    ALU.add).then_inc(resid_ready, 1)

        @block.tensor
        def _(pe):
            pe.wait_ge(q_loaded, 16)
            nc.tensor.matmul(col_ps[:, 0, 0, :], wq_t, x_t, start=True, stop=True).then_inc(q_projected, 1)
            pe.wait_ge(msg_ready, 1)
            nc.tensor.matmul(col_ps[:, 0, 1, :], wk_t, msg_t[:], start=True, stop=True).then_inc(k_projected, 1)
            pe.wait_ge(v_loaded, 16)
            for c in range(CHUNKS):
                last = nc.tensor.matmul(mix_ps[:, c * D:(c + 1) * D], msg_t[:, c * PARTS:(c + 1) * PARTS], wv_t,
                                        start=True, stop=True)
            last.then_inc(v_projected, 1)

            def row_tile(i):
                h, t = divmod(i, TILES)
                if i == 0:
                    pe.wait_ge(stacked, 16 * N_STACKS)
                if i >= 2:
                    pe.wait_ge(rows_maxed, i - 1)
                nc.tensor.matmul(row_ps[:, i % 2, :], queries[0:SCORE_ROWS, h, t * PARTS:(t + 1) * PARTS],
                                 keys[0:SCORE_ROWS, h, :], start=True, stop=True).then_inc(rows_scored, 1)

            def turn_max(h):
                pe.wait_ge(neg_max_ready, h + 1)
                if h == 0:
                    pe.wait_ge(identity_ready, 1)
                if h >= 1:
                    pe.wait_ge(max_rows_ready, h)
                if h == N_HEADS - 1:
                    pe.wait_ge(total_ready, 1)
                for t in range(TILES):
                    last = nc.tensor.matmul(misc_ps[SCORE_ROWS:SHIFTED_ROWS, t * PARTS:(t + 1) * PARTS],
                                            neg_max[:, h, t, :], identity_b[:], start=True, stop=True)
                last.then_inc(max_turned, 1)

            def col_tile(s):
                h, c = divmod(s, CHUNKS)
                pair = s // 2
                if c == 0:
                    pe.wait_ge(max_rows_ready, h + 1)
                if s == 0:
                    pe.wait_ge(ones_ready, 1)
                    pe.wait_ge(bias_cols_ready, 1)
                    pe.wait_ge(q_full_ready, 1)
                    pe.wait_ge(k_full_ready, 1)
                if s % 2 == 0 and pair >= 2:
                    pe.wait_ge(exps_done, pair - 1)
                ps = col_ps[:, pair % 2, s % 2, :]
                nc.tensor.matmul(ps, keys[0:SHIFTED_ROWS, h, c * PARTS:(c + 1) * PARTS],
                                 queries[0:SHIFTED_ROWS, h, :], start=True, stop=False)
                last = nc.tensor.matmul(ps, identity_b[:], bias_cols[:, c, :], start=False, stop=True)
                if s % 2:
                    last.then_inc(cols_scored, 1)

            def mix(g, c):
                pe.wait_ge(exps_done, 2 * (GROUP * (g + 1) - 1) + c // 2 + 1)
                if c == 0 and g == 0:
                    pe.wait_ge(values_ready, 1)
                if c == 0 and g > 0:
                    pe.wait_ge(mixed_copied, g)
                for j in range(GROUP):
                    h = GROUP * g + j
                    last = nc.tensor.matmul(mix_ps[j * LANE:(j + 1) * LANE, :], values[:, c, h, :],
                                            probs[:, h, c, :], start=(c == 0), stop=(c == CHUNKS - 1))
                if c == CHUNKS - 1:
                    last.then_inc(mixed_done, 1)

            def spread_totals(g):
                pe.wait_ge(mixed_copied, g + 1)
                pe.wait_ge(max_rows_ready, N_HEADS if g else N_HEADS - 1)
                nc.tensor.matmul(misc_ps[:], sum_selector, mixed[:, g, :], start=True,
                                 stop=True).then_inc(totals_spread, 1)

            def project_out(g):
                ps = row_ps[:, g, :].rearrange("p (t d) -> p t d", t=TILES)
                pe.wait_ge(mixed_n_ready, g + 1)
                pe.wait_ge(rows_maxed, N_HEADS * TILES)
                for t in range(TILES):
                    nc.tensor.matmul(ps[:, t, :], mixed_n[:, g, t * PARTS:(t + 1) * PARTS], wo_pad[:, g, :],
                                     start=True, stop=True).then_inc(projected_out, 1)

            n_tiles = N_HEADS * TILES
            for i in range(LEAD - 1):
                row_tile(i)
                if i == TILES:
                    turn_max(0)
            for s in range(n_tiles):
                if s + LEAD - 1 < n_tiles:
                    row_tile(s + LEAD - 1)
                if s % CHUNKS == CHUNKS - 1 and s + 1 < n_tiles:
                    turn_max((s + 1) // CHUNKS)
                col_tile(s)
                if s >= 17 and s % 2 and (s - 17) // 2 < CHUNKS:
                    mix(0, (s - 17) // 2)
                if s == 25:
                    spread_totals(0)
            project_out(0)
            for c in range(CHUNKS):
                mix(1, c)
            spread_totals(1)
            project_out(1)

        @block.scalar
        def _(act):
            def high_half(a):
                return a.bitcast(bf16).rearrange("p (t two) -> p t two", two=2)[:, :, 1]

            for ready, full, done, part, n in ((q_full_ready, q_full, q_part_ready, q_part, 0),
                                               (k_full_ready, k_full, k_part_ready, k_part, 0),
                                               (q_rest_ready, q_rest, q_part_ready, q_part, 1),
                                               (k_rest_ready, k_rest, k_part_ready, k_part, 1)):
                act.wait_ge(ready, 1)
                nc.scalar.copy(part[:, n, :], high_half(full[:])).then_inc(done[n], 1)

            def max_rows(h):
                act.wait_ge(max_turned, h + 1)
                nc.scalar.copy(queries[SCORE_ROWS:SHIFTED_ROWS, h, :],
                               misc_ps[SCORE_ROWS:SHIFTED_ROWS, :]).then_inc(max_rows_ready, 1)

            def exp_pair(pair):
                h, half = divmod(pair, 2)
                act.wait_ge(cols_scored, pair + 1)
                nc.scalar.activation(probs[:, h, 2 * half:2 * half + 2, :], col_ps[:, pair % 2, :, :], ACT.Exp,
                                     scale=SCORE_SCALE).then_inc(exps_done, 1)

            def copy_mixed(g):
                act.wait_ge(mixed_done, g + 1)
                nc.scalar.copy(mixed[:, g, :], mix_ps[:]).then_inc(mixed_copied, 1)

            max_rows(0)
            for h in range(N_HEADS):
                exp_pair(2 * h)
                if h + 1 < N_HEADS:
                    max_rows(h + 1)
                exp_pair(2 * h + 1)
                if h == 5:
                    copy_mixed(0)
            copy_mixed(1)
            act.wait_ge(variance_ready, 1)
            nc.scalar.activation(deviation[:], variance[:], ACT.Sqrt).then_inc(deviation_ready, 1)

        @block.vector
        def _(dve):
            def high_half(a):
                return a.bitcast(bf16).rearrange("p (t two) -> p t two", two=2)[:, :, 1]

            dve.wait_ge(k_loaded, 16)
            nc.vector.tensor_scalar(msg_t[:], h_t, edge_col, None, ALU.add).then_inc(msg_ready, 1)
            dve.wait_ge(q_loaded, 16)
            dve.wait_ge(q_projected, 1)
            nc.vector.tensor_scalar(q_full[:], col_ps[:, 0, 0, :], bq_col, None, ALU.add).then_inc(q_full_ready, 1)
            dve.wait_ge(k_projected, 1)
            nc.vector.tensor_scalar(k_full[:], col_ps[:, 0, 1, :], bk_col, None, ALU.add).then_inc(k_full_ready, 1)
            dve.wait_ge(q_full_ready, 1)
            nc.vector.tensor_tensor(q_rest[:], q_full[:], high_half(q_full[:]), ALU.subtract).then_inc(q_rest_ready, 1)
            dve.wait_ge(k_full_ready, 1)
            nc.vector.tensor_tensor(k_rest[:], k_full[:], high_half(k_full[:]), ALU.subtract).then_inc(k_rest_ready, 1)
            dve.wait_ge(q_rest_ready, 1)
            nc.vector.tensor_tensor(q_part[:, 2, :], q_rest[:], high_half(q_rest[:]), ALU.subtract).then_inc(q_part_ready[2], 1)
            dve.wait_ge(k_rest_ready, 1)
            nc.vector.tensor_tensor(k_part[:, 2, :], k_rest[:], high_half(k_rest[:]), ALU.subtract).then_inc(k_part_ready[2], 1)
            dve.wait_ge(adj_rows_loaded, 16)
            nc.vector.tensor_scalar(bias_rows[:], adj_rows[:], 0, MASK_BIAS, ALU.is_equal, ALU.mult).then_inc(bias_rows_ready, 1)
            dve.wait_ge(adj_cols_loaded, 16)
            nc.vector.tensor_scalar(bias_cols[:], adj_cols[:], 0, MASK_BIAS, ALU.is_equal, ALU.mult).then_inc(bias_cols_ready, 1)
            dve.wait_ge(v_projected, 1)
            dve.wait_ge(bv_loaded, 16)
            nc.vector.tensor_tensor(values[:, :, :, 0:D_HEAD],
                                    mix_ps[:].rearrange("p (c h d) -> p c h d", c=CHUNKS, h=N_HEADS),
                                    bv_all[:].rearrange("p (h d) -> p h d", h=N_HEADS).unsqueeze(1)
                                    .to_broadcast([PARTS, CHUNKS, N_HEADS, D_HEAD]),
                                    ALU.add).then_inc(values_ready, 1)
            dve.wait_ge(bias_rows_ready, 1)

            def take_totals(g):
                dve.wait_ge(totals_spread, g + 1)
                nc.vector.tensor_scalar(total[:, g, :], misc_ps[:], TINY, None, ALU.max).then_inc(total_ready, 1)

            def normalise(g):
                dve.wait_ge(total_ready, g + 1)
                nc.vector.reciprocal(per_total[:, g, :], total[:, g, :]).then_inc(per_total_ready, 1)
                dve.wait_ge(mixed_copied, g + 1)
                dve.wait_ge(per_total_ready, g + 1)
                nc.vector.tensor_tensor(mixed_n[:, g, :], mixed[:, g, :], per_total[:, g, :],
                                        ALU.mult).then_inc(mixed_n_ready, 1)

            def cut_max(h):
                dve.wait_ge(rows_maxed, TILES * (h + 1))
                nc.vector.tensor_scalar(neg_max[:, h, :, 0], row_max[:, h, :], -1.0, None, ALU.mult).then_inc(neg_max_high, 1)
                dve.wait_ge(neg_max_high, h + 1)
                nc.vector.scalar_tensor_tensor(neg_max[:, h, :, 1], row_max[:, h, :], -1.0, neg_max[:, h, :, 0],
                                               ALU.mult, ALU.subtract).then_inc(neg_max_ready, 1)

            for i in range(N_HEADS * TILES):
                h, t = divmod(i, TILES)
                dve.wait_ge(rows_scored, i + 1)
                if i >= 4:
                    dve.wait_ge(rows_maxed, i - 3)
                nc.vector.tensor_tensor_reduce(out=masked[:, i % 4, :], in0=row_ps[:, i % 2, :], in1=bias_rows[:, t, :],
                                               scale=1.0, scalar=MAX_FLOOR, op0=ALU.add, op1=ALU.max,
                                               accum_out=row_max[:, h, t:t + 1]).then_inc(rows_maxed, 1)
                if t == TILES - 1:
                    cut_max(h)
                if i == 30:
                    take_totals(0)
            normalise(0)
            dve.wait_ge(resid_ready, 1)
            dve.wait_ge(projected_out, TILES)
            nc.vector.tensor_tensor(resid_0[:], row_ps[:, 0, :].rearrange("p (t d) -> p t d", t=TILES), resid[:],
                                    ALU.add).then_inc(resid_0_ready, 1)
            take_totals(1)
            normalise(1)
            dve.wait_ge(resid_0_ready, 1)
            ps = row_ps[:, 1, :].rearrange("p (t d) -> p t d", t=TILES)
            dve.wait_ge(projected_out, 2 * TILES)
            nc.vector.tensor_tensor(y[:], ps, resid_0[:], ALU.add).then_inc(y_ready, 1)
            dve.wait_ge(y_ready, 1)
            for t in range(TILES):
                nc.vector.bn_stats(stats[:, t, :], y[:, t, :]).then_inc(stats_ready, 1)
            for t in range(TILES):
                dve.wait_ge(stats_ready, t + 1)
                nc.vector.bn_aggr(moments[:, t, :], stats[:, t, :]).then_inc(moments_ready, 1)
            dve.wait_ge(moments_ready, TILES)
            nc.vector.tensor_scalar(variance[:], moments[:, :, 1], EPS, None, ALU.add).then_inc(variance_ready, 1)
            dve.wait_ge(deviation_ready, 1)
            nc.vector.reciprocal(rstd[:], deviation[:]).then_inc(rstd_ready, 1)
            dve.wait_ge(rstd_ready, 1)
            for t in range(TILES):
                nc.vector.tensor_scalar(normed[:, t, :], y[:, t, :], moments[:, t, 0:1], rstd[:, t:t + 1],
                                        ALU.subtract, ALU.mult).then_inc(normed_ready, 1)


def kernel(x, adj, L0_gnn_h_neigh, L0_gnn_Wq, L0_gnn_bq, L0_gnn_Wk, L0_gnn_bk, L0_gnn_Wv, L0_gnn_bv,
           L0_gnn_Wo, L0_gnn_bo, L0_gnn_E):
    import numpy as np
    import concourse.bacc as bacc
    from concourse.bass_utils import run_bass_kernel_spmd

    def dim_major(a):
        return a.reshape(len(a), N_HEADS, D_HEAD).transpose(0, 2, 1).reshape(len(a), D_MODEL)

    x, adj = np.asarray(x), np.asarray(adj)
    wo_t = np.asarray(L0_gnn_Wo).T
    wo_pad = np.zeros((N_GROUPS, GROUP, LANE, D_MODEL), wo_t.dtype)
    wo_pad[:, :, :D_HEAD] = wo_t.reshape(N_GROUPS, GROUP, D_HEAD, D_MODEL)
    wo_pad = wo_pad.reshape(N_GROUPS, PARTS, D_MODEL)
    sum_selector = np.zeros((PARTS, PARTS), wo_t.dtype)
    for j in range(GROUP):
        sum_selector[j * LANE + D_HEAD, j * LANE:(j + 1) * LANE] = 1
    arrays = {
        "q_pack": np.concatenate([x.T, dim_major(np.asarray(L0_gnn_Wq).T), dim_major(np.asarray(L0_gnn_bq)[None, :]).T], 1),
        "k_pack": np.concatenate([np.asarray(L0_gnn_h_neigh).T, dim_major(np.asarray(L0_gnn_Wk).T),
                                  dim_major(np.asarray(L0_gnn_bk)[None, :]).T, np.asarray(L0_gnn_E).T], 1),
        "v_pack": np.concatenate([np.asarray(L0_gnn_Wv).T, wo_pad[0], wo_pad[1], sum_selector,
                                  np.eye(PARTS, dtype=wo_t.dtype)], 1),
        "x": x,
        "adj": adj,
        "adj_t": adj.T,
        "bv": np.asarray(L0_gnn_bv)[None, :],
        "bo": np.asarray(L0_gnn_bo)[None, :],
    }
    arrays = {name: np.ascontiguousarray(a) for name, a in arrays.items()}
    nc = bacc.Bacc("TRN2", target_bir_lowering=False, num_devices=1)
    args = [nc.dram_tensor(name, a.shape, mybir.dt.from_np(a.dtype), kind="ExternalInput").ap()
            for name, a in arrays.items()]
    out = nc.dram_tensor("out", (N_TARGETS, D_MODEL), mybir.dt.float32, kind="ExternalOutput").ap()
    graph_attention(nc, *args, out)
    result = run_bass_kernel_spmd(nc, [arrays], core_ids=[0])
    return result.results[0]["out"]
```

```python
import concourse.bass as bass
from concourse import mybir
from contextlib import ExitStack

PARTS = 128
N_HEADS = 8
D_MODEL = 128
D_HEAD = D_MODEL // N_HEADS
N_TARGETS = 512
N_NEIGHBOURS = 512
TILES = N_TARGETS // PARTS
CHUNKS = N_NEIGHBOURS // PARTS
GROUP = 4
N_GROUPS = N_HEADS // GROUP
LANE = PARTS // GROUP
BLOCK_PARTS = ((0, 0), (0, 1), (1, 0), (1, 1), (0, 2), (2, 0))
SCORE_ROWS = len(BLOCK_PARTS) * D_HEAD
SHIFTED_ROWS = SCORE_ROWS + 2
WARM_START = 7
WARM_PROJECTED = 27
WARM_RAMP = 1
TURN_AT = 5
MASK_BIAS = -float(2 ** 30)
MAX_FLOOR = -float(2 ** 29)
SCORE_SCALE = float(D_HEAD) ** -0.5
TINY = 1e-30
EPS = 1e-5
LEAD = 7


def graph_attention(
    nc: bass.Bass,
    q_pack: bass.AP,
    k_pack: bass.AP,
    v_pack: bass.AP,
    x: bass.AP,
    adj: bass.AP,
    adj_t: bass.AP,
    bv: bass.AP,
    bo: bass.AP,
    out: bass.AP,
):
    fp32 = mybir.dt.float32
    bf16 = mybir.dt.bfloat16
    i32 = mybir.dt.int32
    ALU = mybir.AluOpType
    ACT = mybir.ActivationFunctionType
    T, N, D = N_TARGETS, N_NEIGHBOURS, D_MODEL

    with ExitStack() as ctx:
        def sb(name, shape, dt):
            return ctx.enter_context(nc.sbuf_tensor(name, shape, dt))

        def pb(name, shape):
            return ctx.enter_context(nc.psum_tensor(name, shape, fp32))

        def sem(name):
            return ctx.enter_context(nc.semaphore(name))

        q_in = sb("q_in", [PARTS, T + D + 1], fp32)
        k_in = sb("k_in", [PARTS, N + D + 3], fp32)
        v_in = sb("v_in", [PARTS, D * 3], fp32)
        x_t, wq_t, bq_col = q_in[:, 0:T], q_in[:, T:T + D], q_in[:, T + D:T + D + 1]
        h_t, wk_t, bk_col = k_in[:, 0:N], k_in[:, N:N + D], k_in[:, N + D:N + D + 1]
        edge_col = k_in[:, N + D + 2:N + D + 3]
        wv_t = v_in[:, 0:D]
        wo_t = v_in[:, D:2 * D]
        identity = v_in[:, 2 * D:3 * D]
        x_rows = sb("x_rows", [PARTS, TILES, D], fp32)
        adj_rows = sb("adj_rows", [PARTS, TILES, N], i32)
        adj_cols = sb("adj_cols", [PARTS, CHUNKS, T], i32)
        bv_all = sb("bv_all", [PARTS, D], fp32)
        bo_all = sb("bo_all", [PARTS, D], fp32)
        identity_b = sb("identity_b", [PARTS, PARTS], bf16)
        bias_rows = sb("bias_rows", [PARTS, TILES, N], bf16)
        bias_cols = sb("bias_cols", [PARTS, CHUNKS, T], bf16)
        msg_t = sb("msg_t", [PARTS, N], fp32)
        q_full = sb("q_full", [PARTS, T], fp32)
        k_full = sb("k_full", [PARTS, N], fp32)
        q_rest = sb("q_rest", [PARTS, T], fp32)
        k_rest = sb("k_rest", [PARTS, N], fp32)
        parts = sb("parts", [PARTS, 6, T], bf16)
        stacks = sb("stacks", [PARTS, N_HEADS, 2, T], bf16)
        queries = stacks[:, :, 0, :]
        keys = stacks[:, :, 1, :]
        idle = sb("idle", [PARTS, T], bf16)
        values = sb("values", [PARTS, CHUNKS, N_HEADS, LANE], fp32)
        masked = sb("masked", [PARTS, 4, N], bf16)
        row_max = sb("row_max", [PARTS, N_HEADS, TILES], fp32)
        neg_max = sb("neg_max", [PARTS, N_HEADS, TILES, 2], bf16)
        probs = sb("probs", [PARTS, N_HEADS, CHUNKS, T], fp32)
        mixed = sb("mixed", [PARTS, N_GROUPS, T], fp32)
        total = sb("total", [PARTS, TILES, N_HEADS], fp32)
        per_total = sb("per_total", [PARTS, TILES, N_HEADS], fp32)
        attended = sb("attended", [PARTS, TILES, N_HEADS, D_HEAD], fp32)
        attended_t = sb("attended_t", [PARTS, T], fp32)
        resid = sb("resid", [PARTS, TILES, D], fp32)
        y = sb("y", [PARTS, TILES, D], fp32)
        stats = sb("stats", [PARTS, TILES, 6], fp32)
        moments = sb("moments", [PARTS, TILES, 2], fp32)
        variance = sb("variance", [PARTS, TILES], fp32)
        deviation = sb("deviation", [PARTS, TILES], fp32)
        rstd = sb("rstd", [PARTS, TILES], fp32)
        normed = sb("normed", [PARTS, TILES, D], fp32)

        col_ps = pb("col_ps", [PARTS, 2, 2, T])
        row_ps = pb("row_ps", [PARTS, 2, N])
        mix_ps = pb("mix_ps", [PARTS, T])
        misc_ps = pb("misc_ps", [PARTS, T])

        q_loaded = sem("q_loaded")
        k_loaded = sem("k_loaded")
        v_loaded = sem("v_loaded")
        adj_rows_loaded = sem("adj_rows_loaded")
        adj_cols_loaded = sem("adj_cols_loaded")
        bv_loaded = sem("bv_loaded")
        resid_loaded = sem("resid_loaded")
        msg_ready = sem("msg_ready")
        q_projected = sem("q_projected")
        k_projected = sem("k_projected")
        v_projected = sem("v_projected")
        q_full_ready = sem("q_full_ready")
        k_full_ready = sem("k_full_ready")
        q_rest_ready = sem("q_rest_ready")
        k_rest_ready = sem("k_rest_ready")
        q_parts_ready = sem("q_parts_ready")
        k_parts_ready = sem("k_parts_ready")
        q_last_part_ready = sem("q_last_part_ready")
        k_last_part_ready = sem("k_last_part_ready")
        idle_ready = sem("idle_ready")
        stacked = [sem(f"stacked_{g}") for g in range(N_GROUPS)]
        stacked_by_pool = [sem(f"stacked_by_pool_{g}") for g in range(N_GROUPS)]
        ones_ready = sem("ones_ready")
        value_ones_ready = sem("value_ones_ready")
        values_ready = sem("values_ready")
        identity_ready = sem("identity_ready")
        bias_rows_ready = sem("bias_rows_ready")
        bias_cols_ready = sem("bias_cols_ready")
        rows_scored = sem("rows_scored")
        rows_maxed = sem("rows_maxed")
        neg_max_high = sem("neg_max_high")
        neg_max_ready = sem("neg_max_ready")
        max_turned = sem("max_turned")
        max_rows_ready = sem("max_rows_ready")
        cols_scored = sem("cols_scored")
        exps_done = sem("exps_done")
        mixed_done = sem("mixed_done")
        mixed_copied = sem("mixed_copied")
        mixed_turned = sem("mixed_turned")
        total_ready = sem("total_ready")
        per_total_ready = sem("per_total_ready")
        attended_ready = sem("attended_ready")
        attended_turned = sem("attended_turned")
        attended_t_ready = sem("attended_t_ready")
        resid_ready = sem("resid_ready")
        projected_out = sem("projected_out")
        y_ready = sem("y_ready")
        stats_ready = sem("stats_ready")
        moments_ready = sem("moments_ready")
        variance_ready = sem("variance_ready")
        deviation_ready = sem("deviation_ready")
        rstd_ready = sem("rstd_ready")
        normed_ready = sem("normed_ready")
        stored = sem("stored")

        def high_half(a):
            return a.bitcast(bf16).rearrange("p (t two) -> p t two", two=2)[:, :, 1]

        def stack(eng, g, b, done):
            q_slot, k_slot = BLOCK_PARTS[b][0], 3 + BLOCK_PARTS[b][1]
            eng.dma_start(stacks[D_HEAD * b:D_HEAD * (b + 1), GROUP * g:GROUP * (g + 1), :, :],
                          parts[PARTS // N_GROUPS * g:PARTS // N_GROUPS * (g + 1),
                                q_slot:k_slot + 1:k_slot - q_slot, :]).then_inc(done, 16)

        block = ctx.enter_context(nc.Block())

        @block.sync
        def _(sp):
            sp.dma_start(q_in[:], q_pack).then_inc(q_loaded, 16)
            sp.dma_start(k_in[:], k_pack).then_inc(k_loaded, 16)
            sp.dma_start(adj_rows[:], adj.rearrange("(t p) n -> p t n", p=PARTS)).then_inc(adj_rows_loaded, 16)
            sp.dma_start(adj_cols[:], adj_t.rearrange("(c p) t -> p c t", p=PARTS)).then_inc(adj_cols_loaded, 16)
            sp.dma_start(x_rows[:], x.rearrange("(t p) d -> p t d", p=PARTS)).then_inc(resid_loaded, 16)
            sp.dma_start(bo_all[:], bo.to_broadcast([PARTS, D])).then_inc(resid_loaded, 16)
            for g in range(N_GROUPS):
                if g == 0:
                    sp.wait_ge(q_parts_ready, 1)
                    sp.wait_ge(k_parts_ready, 1)
                stack(sp, g, 0, stacked[g])
                if g == 0:
                    sp.wait_ge(q_parts_ready, 2)
                stack(sp, g, 2, stacked[g])
                if g == 0:
                    sp.wait_ge(q_last_part_ready, 1)
                stack(sp, g, 5, stacked[g])
                if g == 0:
                    sp.wait_ge(k_last_part_ready, 1)
                stack(sp, g, 4, stacked[g])
            for half in range(2):
                sp.wait_ge(normed_ready, 2 * (half + 1))
                sp.dma_start(out[half * T // 2:(half + 1) * T // 2, :].rearrange("(t p) d -> p t d", p=PARTS),
                             normed[:, 2 * half:2 * half + 2, :]).then_inc(stored, 16)
            sp.wait_ge(stored, 32)

        @block.gpsimd
        def _(pool):
            pool.dma_start(v_in[:], v_pack).then_inc(v_loaded, 16)
            pool.dma_start(bv_all[:], bv.to_broadcast([PARTS, D])).then_inc(bv_loaded, 16)
            nc.gpsimd.memset(stacks[SCORE_ROWS:SHIFTED_ROWS, :, 1, :], 1.0).then_inc(ones_ready, 1)
            pool.wait_ge(ones_ready, 1)
            nc.gpsimd.memset(values[:, :, :, D_HEAD:LANE], 1.0).then_inc(value_ones_ready, 1)
            pool.wait_ge(v_loaded, 16)
            pool.wait_ge(value_ones_ready, 1)
            nc.gpsimd.tensor_copy(identity_b[:], identity).then_inc(identity_ready, 1)
            pool.wait_ge(q_parts_ready, 2)
            pool.wait_ge(k_parts_ready, 2)
            for g in range(N_GROUPS):
                for b in (1, 3):
                    stack(pool, g, b, stacked_by_pool[g])
            pool.wait_ge(identity_ready, 1)
            pool.wait_ge(resid_loaded, 32)
            nc.gpsimd.tensor_tensor(resid[:], x_rows[:],
                                    bo_all[:].unsqueeze(1).to_broadcast([PARTS, TILES, D]),
                                    ALU.add).then_inc(resid_ready, 1)

        @block.tensor
        def _(pe):
            def keep_warm(ps, n):
                for _ in range(n):
                    nc.tensor.matmul(ps[:], idle[:, 0:PARTS], idle[:], start=True, stop=True)

            pe.wait_ge(idle_ready, 1)
            keep_warm(misc_ps, WARM_START)
            pe.wait_ge(q_loaded, 16)
            nc.tensor.matmul(col_ps[:, 0, 0, :], wq_t, x_t, start=True, stop=True).then_inc(q_projected, 1)
            pe.wait_ge(msg_ready, 1)
            nc.tensor.matmul(col_ps[:, 0, 1, :], wk_t, msg_t[:], start=True, stop=True).then_inc(k_projected, 1)
            pe.wait_ge(v_loaded, 16)
            for c in range(CHUNKS):
                last = nc.tensor.matmul(mix_ps[:, c * D:(c + 1) * D], msg_t[:, c * PARTS:(c + 1) * PARTS], wv_t,
                                        start=True, stop=True)
            last.then_inc(v_projected, 1)
            keep_warm(misc_ps, WARM_PROJECTED)

            def row_tile(i):
                h, t = divmod(i, TILES)
                if h % GROUP == 0 and t == 0:
                    pe.wait_ge(stacked[h // GROUP], 16 * 4)
                    pe.wait_ge(stacked_by_pool[h // GROUP], 16 * 2)
                if i >= 2:
                    pe.wait_ge(rows_maxed, i - 1)
                nc.tensor.matmul(row_ps[:, i % 2, :], queries[0:SCORE_ROWS, h, t * PARTS:(t + 1) * PARTS],
                                 keys[0:SCORE_ROWS, h, :], start=True, stop=True).then_inc(rows_scored, 1)

            def turn_max(h):
                pe.wait_ge(neg_max_ready, h + 1)
                if h == 0:
                    pe.wait_ge(identity_ready, 1)
                if h >= 1:
                    pe.wait_ge(max_rows_ready, h)
                for t in range(TILES):
                    last = nc.tensor.matmul(misc_ps[SCORE_ROWS:SHIFTED_ROWS, t * PARTS:(t + 1) * PARTS],
                                            neg_max[:, h, t, :], identity_b[:], start=True, stop=True)
                last.then_inc(max_turned, 1)

            def col_tile(s):
                h, c = divmod(s, CHUNKS)
                pair = s // 2
                if c == 0:
                    pe.wait_ge(max_rows_ready, h + 1)
                if s == 0:
                    pe.wait_ge(ones_ready, 1)
                    pe.wait_ge(bias_cols_ready, 1)
                    pe.wait_ge(q_full_ready, 1)
                    pe.wait_ge(k_full_ready, 1)
                if s % 2 == 0 and pair >= 2:
                    pe.wait_ge(exps_done, pair - 1)
                ps = col_ps[:, pair % 2, s % 2, :]
                nc.tensor.matmul(ps, keys[0:SHIFTED_ROWS, h, c * PARTS:(c + 1) * PARTS],
                                 queries[0:SHIFTED_ROWS, h, :], start=True, stop=False)
                last = nc.tensor.matmul(ps, identity_b[:], bias_cols[:, c, :], start=False, stop=True)
                if s % 2:
                    last.then_inc(cols_scored, 1)

            def mix(g, c):
                pe.wait_ge(exps_done, 2 * (GROUP * (g + 1) - 1) + c // 2 + 1)
                if c == 0 and g == 0:
                    pe.wait_ge(values_ready, 1)
                if c == 0 and g > 0:
                    pe.wait_ge(attended_ready, 1)
                for j in range(GROUP):
                    h = GROUP * g + j
                    last = nc.tensor.matmul(mix_ps[j * LANE:(j + 1) * LANE, :], values[:, c, h, :],
                                            probs[:, h, c, :], start=(c == 0), stop=(c == CHUNKS - 1))
                if c == CHUNKS - 1:
                    last.then_inc(mixed_done, 1)

            def turn_mixed(ps, g, tiles):
                for n, t in enumerate(tiles):
                    last = nc.tensor.transpose(ps[:, n * PARTS:(n + 1) * PARTS],
                                               mixed[:, g, t * PARTS:(t + 1) * PARTS], identity)
                last.then_inc(mixed_turned, 1)

            n_tiles = N_HEADS * TILES
            for i in range(LEAD - 1):
                row_tile(i)
                if i == TURN_AT:
                    turn_max(0)
                if i == 0:
                    pe.wait_ge(values_ready, 1)
                keep_warm(mix_ps, WARM_RAMP)
            for s in range(n_tiles):
                if s + LEAD - 1 < n_tiles:
                    row_tile(s + LEAD - 1)
                if s % CHUNKS == CHUNKS - 1 and s + 1 < n_tiles:
                    turn_max((s + 1) // CHUNKS)
                col_tile(s)
                if s >= 17 and s % 2 and (s - 17) // 2 < CHUNKS:
                    mix(0, (s - 17) // 2)
                if s == 25:
                    pe.wait_ge(mixed_copied, 1)
                    turn_mixed(mix_ps[:], 0, range(TILES))
            for c in range(CHUNKS):
                mix(1, c)
            pe.wait_ge(exps_done, 2 * N_HEADS)
            pe.wait_ge(rows_maxed, N_HEADS * TILES)
            for half in range(2):
                pe.wait_ge(mixed_copied, 2 + half)
                turn_mixed(col_ps[:, 0, half, :], 1, (2 * half, 2 * half + 1))
            for half in range(2):
                pe.wait_ge(attended_ready, 2 + half)
                for n in range(2):
                    t = 2 * half + n
                    last = nc.tensor.transpose(col_ps[:, 1, half, n * PARTS:(n + 1) * PARTS],
                                               attended[:, t, :, :].rearrange("p h d -> p (h d)"), identity)
                last.then_inc(attended_turned, 1)
            for half in range(2):
                pe.wait_ge(attended_t_ready, half + 1)
                for n in range(2):
                    t = 2 * half + n
                    last = nc.tensor.matmul(row_ps[:, half, n * D:(n + 1) * D],
                                            attended_t[:, t * PARTS:(t + 1) * PARTS], wo_t, start=True, stop=True)
                last.then_inc(projected_out, 1)

        @block.scalar
        def _(act):
            for ready, full, done, slot in ((q_full_ready, q_full, q_parts_ready, 0),
                                            (q_rest_ready, q_rest, q_parts_ready, 1),
                                            (k_full_ready, k_full, k_parts_ready, 3),
                                            (k_rest_ready, k_rest, k_parts_ready, 4)):
                act.wait_ge(ready, 1)
                nc.scalar.copy(parts[:, slot, :], high_half(full[:])).then_inc(done, 1)

            def max_rows(h):
                act.wait_ge(max_turned, h + 1)
                nc.scalar.copy(queries[SCORE_ROWS:SHIFTED_ROWS, h, :],
                               misc_ps[SCORE_ROWS:SHIFTED_ROWS, :]).then_inc(max_rows_ready, 1)

            def exp_pair(pair):
                h, half = divmod(pair, 2)
                act.wait_ge(cols_scored, pair + 1)
                nc.scalar.activation(probs[:, h, 2 * half:2 * half + 2, :], col_ps[:, pair % 2, :, :], ACT.Exp,
                                     scale=SCORE_SCALE).then_inc(exps_done, 1)

            max_rows(0)
            for h in range(N_HEADS):
                exp_pair(2 * h)
                if h + 1 < N_HEADS:
                    max_rows(h + 1)
                exp_pair(2 * h + 1)
                if h == 5:
                    act.wait_ge(mixed_done, 1)
                    nc.scalar.copy(mixed[:, 0, :], mix_ps[:]).then_inc(mixed_copied, 1)
            nc.scalar.preload_act_table(ACT.Sqrt)
            act.wait_ge(mixed_done, 2)
            for half in range(2):
                cols = slice(half * T // 2, (half + 1) * T // 2)
                nc.scalar.copy(mixed[:, 1, cols], mix_ps[:, cols]).then_inc(mixed_copied, 1)
            for half in range(2):
                act.wait_ge(attended_turned, half + 1)
                nc.scalar.copy(attended_t[:, half * T // 2:(half + 1) * T // 2],
                               col_ps[:, 1, half, 0:T // 2]).then_inc(attended_t_ready, 1)
            for half in range(2):
                act.wait_ge(variance_ready, half + 1)
                nc.scalar.activation(deviation[:, 2 * half:2 * half + 2], variance[:, 2 * half:2 * half + 2],
                                     ACT.Sqrt).then_inc(deviation_ready, 1)

        @block.vector
        def _(dve):
            nc.vector.memset(idle[:], 0.0).then_inc(idle_ready, 1)
            dve.wait_ge(k_loaded, 16)
            nc.vector.tensor_scalar(msg_t[:], h_t, edge_col, None, ALU.add).then_inc(msg_ready, 1)
            dve.wait_ge(q_loaded, 16)
            dve.wait_ge(q_projected, 1)
            nc.vector.tensor_scalar(q_full[:], col_ps[:, 0, 0, :], bq_col, None, ALU.add).then_inc(q_full_ready, 1)
            dve.wait_ge(q_full_ready, 1)
            nc.vector.tensor_tensor(q_rest[:], q_full[:], high_half(q_full[:]), ALU.subtract).then_inc(q_rest_ready, 1)
            dve.wait_ge(k_projected, 1)
            nc.vector.tensor_scalar(k_full[:], col_ps[:, 0, 1, :], bk_col, None, ALU.add).then_inc(k_full_ready, 1)
            dve.wait_ge(k_full_ready, 1)
            nc.vector.tensor_tensor(k_rest[:], k_full[:], high_half(k_full[:]), ALU.subtract).then_inc(k_rest_ready, 1)
            dve.wait_ge(q_rest_ready, 1)
            nc.vector.tensor_tensor(parts[:, 2, :], q_rest[:], high_half(q_rest[:]),
                                    ALU.subtract).then_inc(q_last_part_ready, 1)
            dve.wait_ge(k_rest_ready, 1)
            nc.vector.tensor_tensor(parts[:, 5, :], k_rest[:], high_half(k_rest[:]),
                                    ALU.subtract).then_inc(k_last_part_ready, 1)
            dve.wait_ge(adj_rows_loaded, 16)
            nc.vector.tensor_scalar(bias_rows[:], adj_rows[:], 0, MASK_BIAS, ALU.is_equal, ALU.mult).then_inc(bias_rows_ready, 1)
            dve.wait_ge(adj_cols_loaded, 16)
            nc.vector.tensor_scalar(bias_cols[:], adj_cols[:], 0, MASK_BIAS, ALU.is_equal, ALU.mult).then_inc(bias_cols_ready, 1)
            dve.wait_ge(v_projected, 1)
            dve.wait_ge(bv_loaded, 16)
            nc.vector.tensor_tensor(values[:, :, :, 0:D_HEAD],
                                    mix_ps[:].rearrange("p (c h d) -> p c h d", c=CHUNKS, h=N_HEADS),
                                    bv_all[:].rearrange("p (h d) -> p h d", h=N_HEADS).unsqueeze(1)
                                    .to_broadcast([PARTS, CHUNKS, N_HEADS, D_HEAD]),
                                    ALU.add).then_inc(values_ready, 1)
            dve.wait_ge(bias_rows_ready, 1)

            def normalise(n, ps, g, tiles):
                heads = slice(GROUP * g, GROUP * (g + 1))
                t = slice(tiles[0], tiles[-1] + 1)
                ps = ps.rearrange("p (t h d) -> p t h d", t=len(tiles), h=GROUP)
                dve.wait_ge(mixed_turned, n + 1)
                nc.vector.tensor_scalar(total[:, t, heads], ps[:, :, :, D_HEAD], TINY, None,
                                        ALU.max).then_inc(total_ready, 1)
                dve.wait_ge(total_ready, n + 1)
                nc.vector.reciprocal(per_total[:, t, heads], total[:, t, heads]).then_inc(per_total_ready, 1)
                dve.wait_ge(per_total_ready, n + 1)
                nc.vector.tensor_tensor(attended[:, t, heads, :], ps[:, :, :, 0:D_HEAD],
                                        per_total[:, t, heads].unsqueeze(3)
                                        .to_broadcast([PARTS, len(tiles), GROUP, D_HEAD]),
                                        ALU.mult).then_inc(attended_ready, 1)

            def cut_max(h):
                dve.wait_ge(rows_maxed, TILES * (h + 1))
                nc.vector.tensor_scalar(neg_max[:, h, :, 0], row_max[:, h, :], -1.0, None, ALU.mult).then_inc(neg_max_high, 1)
                dve.wait_ge(neg_max_high, h + 1)
                nc.vector.scalar_tensor_tensor(neg_max[:, h, :, 1], row_max[:, h, :], -1.0, neg_max[:, h, :, 0],
                                               ALU.mult, ALU.subtract).then_inc(neg_max_ready, 1)

            for i in range(N_HEADS * TILES):
                h, t = divmod(i, TILES)
                dve.wait_ge(rows_scored, i + 1)
                if i >= 4:
                    dve.wait_ge(rows_maxed, i - 3)
                nc.vector.tensor_tensor_reduce(out=masked[:, i % 4, :], in0=row_ps[:, i % 2, :], in1=bias_rows[:, t, :],
                                               scale=1.0, scalar=MAX_FLOOR, op0=ALU.add, op1=ALU.max,
                                               accum_out=row_max[:, h, t:t + 1]).then_inc(rows_maxed, 1)
                if t == TILES - 1:
                    cut_max(h)
            normalise(0, mix_ps[:], 0, range(TILES))
            for half in range(2):
                normalise(1 + half, col_ps[:, 0, half, 0:T // 2], 1, (2 * half, 2 * half + 1))
            dve.wait_ge(resid_ready, 1)
            for half in range(2):
                tiles = slice(2 * half, 2 * half + 2)
                dve.wait_ge(projected_out, half + 1)
                nc.vector.tensor_tensor(y[:, tiles, :], row_ps[:, half, 0:2 * D].rearrange("p (t d) -> p t d", t=2),
                                        resid[:, tiles, :], ALU.add).then_inc(y_ready, 1)
                dve.wait_ge(y_ready, half + 1)
                for t in (2 * half, 2 * half + 1):
                    nc.vector.bn_stats(stats[:, t, :], y[:, t, :]).then_inc(stats_ready, 1)
                for t in (2 * half, 2 * half + 1):
                    dve.wait_ge(stats_ready, t + 1)
                    nc.vector.bn_aggr(moments[:, t, :], stats[:, t, :]).then_inc(moments_ready, 1)
                dve.wait_ge(moments_ready, 2 * half + 2)
                nc.vector.tensor_scalar(variance[:, tiles], moments[:, tiles, 1], EPS, None,
                                        ALU.add).then_inc(variance_ready, 1)
            for half in range(2):
                tiles = slice(2 * half, 2 * half + 2)
                dve.wait_ge(deviation_ready, half + 1)
                nc.vector.reciprocal(rstd[:, tiles], deviation[:, tiles]).then_inc(rstd_ready, 1)
                dve.wait_ge(rstd_ready, half + 1)
                for t in (2 * half, 2 * half + 1):
                    nc.vector.tensor_scalar(normed[:, t, :], y[:, t, :], moments[:, t, 0:1], rstd[:, t:t + 1],
                                            ALU.subtract, ALU.mult).then_inc(normed_ready, 1)


def kernel(x, adj, L0_gnn_h_neigh, L0_gnn_Wq, L0_gnn_bq, L0_gnn_Wk, L0_gnn_bk, L0_gnn_Wv, L0_gnn_bv,
           L0_gnn_Wo, L0_gnn_bo, L0_gnn_E):
    import numpy as np
    import concourse.bacc as bacc
    from concourse.bass_utils import run_bass_kernel_spmd

    def dim_major(a):
        return a.reshape(len(a), N_GROUPS, GROUP, D_HEAD).transpose(0, 1, 3, 2).reshape(len(a), D_MODEL)

    x, adj = np.asarray(x), np.asarray(adj)
    arrays = {
        "q_pack": np.concatenate([x.T, dim_major(np.asarray(L0_gnn_Wq).T), dim_major(np.asarray(L0_gnn_bq)[None, :]).T], 1),
        "k_pack": np.concatenate([np.asarray(L0_gnn_h_neigh).T, dim_major(np.asarray(L0_gnn_Wk).T),
                                  dim_major(np.asarray(L0_gnn_bk)[None, :]).T, np.asarray(L0_gnn_E).T], 1),
        "v_pack": np.concatenate([np.asarray(L0_gnn_Wv).T, np.asarray(L0_gnn_Wo).T,
                                  np.eye(PARTS, dtype=np.float32)], 1),
        "x": x,
        "adj": adj,
        "adj_t": adj.T,
        "bv": np.asarray(L0_gnn_bv)[None, :],
        "bo": np.asarray(L0_gnn_bo)[None, :],
    }
    arrays = {name: np.ascontiguousarray(a) for name, a in arrays.items()}
    nc = bacc.Bacc("TRN2", target_bir_lowering=False, num_devices=1)
    args = [nc.dram_tensor(name, a.shape, mybir.dt.from_np(a.dtype), kind="ExternalInput").ap()
            for name, a in arrays.items()]
    out = nc.dram_tensor("out", (N_TARGETS, D_MODEL), mybir.dt.float32, kind="ExternalOutput").ap()
    graph_attention(nc, *args, out)
    result = run_bass_kernel_spmd(nc, [arrays], core_ids=[0])
    return result.results[0]["out"]
```

```python
import concourse.bass as bass
from concourse import mybir
from contextlib import ExitStack

PARTS = 128
N_HEADS = 8
D_MODEL = 128
D_HEAD = D_MODEL // N_HEADS
N_TARGETS = 512
N_NEIGHBOURS = 512
TILES = N_TARGETS // PARTS
CHUNKS = N_NEIGHBOURS // PARTS
GROUP = 4
N_GROUPS = N_HEADS // GROUP
LANE = PARTS // GROUP
BLOCK_PARTS = ((0, 0), (0, 1), (1, 0), (1, 1), (0, 2), (2, 0))
SCORE_ROWS = len(BLOCK_PARTS) * D_HEAD
SHIFTED_ROWS = SCORE_ROWS + 2
WARM_START = 6
WARM_PROJECTED = 20
WARM_RAMP = 1
MASK_BIAS = -float(2 ** 30)
NEG_MAX_CEILING = float(2 ** 29)
SCORE_SCALE = float(D_HEAD) ** -0.5
TINY = 1e-30
LARGEST = 3e38
EPS = 1e-5
POOL_TILES = tuple(range(1, 28, 2))
DVE_TILES = (20, 22, 24, 26, 28, 29)
LEAD = 8
MIX_AFTER = (19, 23, 25, 27)
COPY_AFTER = 28
TURN_FIRST_AT = 5
MAX_ROWS_AFTER = 1
ROW_BANKS = 3
COL_BANKS = 3
MASKED_SLOTS = 4


def graph_attention(
    nc: bass.Bass,
    q_pack: bass.AP,
    k_pack: bass.AP,
    v_pack: bass.AP,
    x: bass.AP,
    adj: bass.AP,
    adj_t: bass.AP,
    bv: bass.AP,
    bo: bass.AP,
    out: bass.AP,
):
    fp32 = mybir.dt.float32
    bf16 = mybir.dt.bfloat16
    i32 = mybir.dt.int32
    ALU = mybir.AluOpType
    ACT = mybir.ActivationFunctionType
    T, N, D = N_TARGETS, N_NEIGHBOURS, D_MODEL

    with ExitStack() as ctx:
        def sb(name, shape, dt):
            return ctx.enter_context(nc.sbuf_tensor(name, shape, dt))

        def pb(name, shape):
            return ctx.enter_context(nc.psum_tensor(name, shape, fp32))

        def sem(name):
            return ctx.enter_context(nc.semaphore(name))

        q_in = sb("q_in", [PARTS, T + D + 1], fp32)
        k_in = sb("k_in", [PARTS, N + D + 3], fp32)
        v_in = sb("v_in", [PARTS, D * 3], fp32)
        x_t, wq_t, bq_col = q_in[:, 0:T], q_in[:, T:T + D], q_in[:, T + D:T + D + 1]
        h_t, wk_t, bk_col = k_in[:, 0:N], k_in[:, N:N + D], k_in[:, N + D:N + D + 1]
        edge_col = k_in[:, N + D + 2:N + D + 3]
        wv_t = v_in[:, 0:D]
        wo_t = v_in[:, D:2 * D]
        identity = v_in[:, 2 * D:3 * D]
        x_rows = sb("x_rows", [PARTS, TILES, D], fp32)
        adj_rows = sb("adj_rows", [PARTS, TILES, N], i32)
        adj_cols = sb("adj_cols", [PARTS, CHUNKS, T], i32)
        bv_row = sb("bv_row", [1, D], fp32)
        ones_row = sb("ones_row", [1, PARTS], fp32)
        bo_all = sb("bo_all", [PARTS, D], fp32)
        identity_b = sb("identity_b", [PARTS, PARTS], bf16)
        bias_rows = sb("bias_rows", [PARTS, TILES, N], bf16)
        bias_cols = sb("bias_cols", [PARTS, CHUNKS, T], bf16)
        edges_cols = sb("edges_cols", [PARTS, CHUNKS, T], i32)
        msg_t = sb("msg_t", [PARTS, N], fp32)
        q_rest = sb("q_rest", [PARTS, T], fp32)
        k_rest = sb("k_rest", [PARTS, N], fp32)
        parts = sb("parts", [PARTS, 6, T], bf16)
        stacks = sb("stacks", [PARTS, N_HEADS, 2, T], bf16)
        queries = stacks[:, :, 0, :]
        keys = stacks[:, :, 1, :]
        idle = sb("idle", [PARTS, T], bf16)
        values = sb("values", [PARTS, CHUNKS, N_HEADS, LANE], fp32)
        masked = sb("masked", [PARTS, MASKED_SLOTS, N], bf16)
        neg_max = sb("neg_max", [PARTS, N_HEADS, TILES, 2], fp32)
        neg_max_halves = neg_max[:].rearrange("p h t w -> p (h t w)").bitcast(bf16).rearrange(
            "p (h t w) -> p h t w", h=N_HEADS, t=TILES)
        neg_max_parts = neg_max_halves[:, :, :, 1:4:2]
        probs = sb("probs", [PARTS, N_HEADS, CHUNKS, T], fp32)
        mixed = sb("mixed", [PARTS, N_GROUPS, T], fp32)
        total = sb("total", [PARTS, TILES, N_HEADS], fp32)
        per_total = sb("per_total", [PARTS, TILES, N_HEADS], fp32)
        attended = sb("attended", [PARTS, TILES, N_HEADS, D_HEAD], fp32)
        attended_t = sb("attended_t", [PARTS, T], fp32)
        resid = sb("resid", [PARTS, TILES, D], fp32)
        stats = sb("stats", [PARTS, TILES, 6], fp32)
        moments = sb("moments", [PARTS, TILES, 2], fp32)
        deviation = sb("deviation", [PARTS, TILES], fp32)
        rstd = sb("rstd", [PARTS, TILES], fp32)
        minus_mean = sb("minus_mean", [PARTS, 2], fp32)
        normed = sb("normed", [PARTS, TILES, D], fp32)

        col_ps = pb("col_ps", [PARTS, COL_BANKS, T])
        row_ps = pb("row_ps", [PARTS, ROW_BANKS, N])
        mix_ps = pb("mix_ps", [PARTS, T])
        misc_ps = pb("misc_ps", [PARTS, T])

        mixed_ps = ((mix_ps[:],), (row_ps[:, 0, 0:T // 2], row_ps[:, 1, 0:T // 2]))
        y_ps = (misc_ps[:, 0:D], mix_ps[:, 0:D], row_ps[:, 0, 0:D], row_ps[:, 1, 0:D])
        turned_ps = (col_ps[:, 2, :], row_ps[:, 2, :])

        q_loaded = sem("q_loaded")
        k_loaded = sem("k_loaded")
        v_loaded = sem("v_loaded")
        adj_rows_loaded = sem("adj_rows_loaded")
        adj_cols_loaded = sem("adj_cols_loaded")
        bv_loaded = sem("bv_loaded")
        resid_loaded = sem("resid_loaded")
        msg_ready = sem("msg_ready")
        q_projected = sem("q_projected")
        k_projected = sem("k_projected")
        v_projected = sem("v_projected")
        q_first_part_ready = sem("q_first_part_ready")
        k_first_part_ready = sem("k_first_part_ready")
        q_middle_part_ready = sem("q_middle_part_ready")
        k_middle_part_ready = sem("k_middle_part_ready")
        q_rest_ready = sem("q_rest_ready")
        k_rest_ready = sem("k_rest_ready")
        q_last_part_ready = sem("q_last_part_ready")
        k_last_part_ready = sem("k_last_part_ready")
        idle_ready = sem("idle_ready")
        stacked = [sem(f"stacked_{g}") for g in range(N_GROUPS)]
        stacked_by_pool = [sem(f"stacked_by_pool_{g}") for g in range(N_GROUPS)]
        ones_ready = sem("ones_ready")
        ones_row_ready = sem("ones_row_ready")
        value_ones_ready = sem("value_ones_ready")
        values_ready = sem("values_ready")
        identity_ready = sem("identity_ready")
        bias_rows_ready = sem("bias_rows_ready")
        bias_cols_ready = sem("bias_cols_ready")
        rows_scored = sem("rows_scored")
        rows_maxed = sem("rows_maxed")
        neg_max_ready = sem("neg_max_ready")
        max_turned = sem("max_turned")
        max_rows_ready = sem("max_rows_ready")
        edges_cols_ready = sem("edges_cols_ready")
        edges_kept_by_pool = sem("edges_kept_by_pool")
        cols_scored = sem("cols_scored")
        exps_done = sem("exps_done")
        mixed_done = sem("mixed_done")
        mixed_copied = sem("mixed_copied")
        mixed_turned = sem("mixed_turned")
        total_ready = sem("total_ready")
        per_total_ready = sem("per_total_ready")
        attended_ready = sem("attended_ready")
        attended_turned = sem("attended_turned")
        attended_t_ready = sem("attended_t_ready")
        resid_ready = sem("resid_ready")
        projected_out = sem("projected_out")
        stats_ready = sem("stats_ready")
        moments_ready = sem("moments_ready")
        deviation_ready = sem("deviation_ready")
        rstd_ready = sem("rstd_ready")
        normed_by_act = sem("normed_by_act")
        minus_mean_ready = sem("minus_mean_ready")
        normed_ready = sem("normed_ready")
        edges_kept_by_dve = sem("edges_kept_by_dve")
        stored = sem("stored")

        def stack(eng, g, b, done):
            q_slot, k_slot = BLOCK_PARTS[b][0], 3 + BLOCK_PARTS[b][1]
            eng.dma_start(stacks[D_HEAD * b:D_HEAD * (b + 1), GROUP * g:GROUP * (g + 1), :, :],
                          parts[PARTS // N_GROUPS * g:PARTS // N_GROUPS * (g + 1),
                                q_slot:k_slot + 1:k_slot - q_slot, :]).then_inc(done, 16)

        block = ctx.enter_context(nc.Block())

        @block.sync
        def _(sp):
            sp.dma_start(q_in[:], q_pack).then_inc(q_loaded, 16)
            sp.dma_start(k_in[:], k_pack).then_inc(k_loaded, 16)
            sp.dma_start(bv_row[:], bv).then_inc(bv_loaded, 16)
            sp.dma_start(adj_rows[:], adj.rearrange("(t p) n -> p t n", p=PARTS)).then_inc(adj_rows_loaded, 16)
            sp.dma_start(adj_cols[:], adj_t.rearrange("(c p) t -> p c t", p=PARTS)).then_inc(adj_cols_loaded, 16)
            for g in range(N_GROUPS):
                if g == 0:
                    sp.wait_ge(q_first_part_ready, 1)
                    sp.wait_ge(k_first_part_ready, 1)
                stack(sp, g, 0, stacked[g])
                if g == 0:
                    sp.wait_ge(k_middle_part_ready, 1)
                stack(sp, g, 1, stacked[g])
                if g == 0:
                    sp.wait_ge(q_middle_part_ready, 1)
                stack(sp, g, 3, stacked[g])
                if g == 0:
                    sp.wait_ge(k_last_part_ready, 1)
                stack(sp, g, 4, stacked[g])
            sp.dma_start(x_rows[:], x.rearrange("(t p) d -> p t d", p=PARTS)).then_inc(resid_loaded, 16)
            sp.dma_start(bo_all[:], bo.to_broadcast([PARTS, D])).then_inc(resid_loaded, 16)
            for half in range(2):
                sp.wait_ge((normed_by_act, normed_ready)[half], 2)
                sp.dma_start(out[half * T // 2:(half + 1) * T // 2, :].rearrange("(t p) d -> p t d", p=PARTS),
                             normed[:, 2 * half:2 * half + 2, :]).then_inc(stored, 16)
            sp.wait_ge(stored, 32)

        @block.gpsimd
        def _(pool):
            pool.dma_start(v_in[:], v_pack).then_inc(v_loaded, 16)
            nc.gpsimd.memset(stacks[SCORE_ROWS:SHIFTED_ROWS, :, 1, :], 1.0).then_inc(ones_ready, 1)
            pool.wait_ge(ones_ready, 1)
            nc.gpsimd.memset(values[:, :, :, D_HEAD:LANE], 1.0).then_inc(value_ones_ready, 1)
            pool.wait_ge(v_loaded, 16)
            pool.wait_ge(value_ones_ready, 1)
            nc.gpsimd.tensor_copy(identity_b[:], identity).then_inc(identity_ready, 1)
            for g in range(N_GROUPS):
                if g == 0:
                    pool.wait_ge(q_middle_part_ready, 1)
                    pool.wait_ge(k_first_part_ready, 1)
                if g == 1:
                    pool.wait_ge(k_last_part_ready, 1)
                stack(pool, g, 2, stacked_by_pool[g])
                if g == 0:
                    pool.wait_ge(q_last_part_ready, 1)
                stack(pool, g, 5, stacked_by_pool[g])
            pool.wait_ge(identity_ready, 1)
            pool.wait_ge(edges_cols_ready, 1)
            for n, s in enumerate(POOL_TILES):
                h, c = divmod(s, CHUNKS)
                words = probs[:, h, c, :].bitcast(i32)
                pool.wait_ge(exps_done, s + 1)
                if n:
                    pool.wait_ge(edges_kept_by_pool, n)
                nc.gpsimd.tensor_tensor(words, words, edges_cols[:, c, :], ALU.mult).then_inc(edges_kept_by_pool, 1)
            pool.wait_ge(edges_kept_by_pool, len(POOL_TILES))
            pool.wait_ge(resid_loaded, 32)
            nc.gpsimd.tensor_tensor(resid[:], x_rows[:],
                                    bo_all[:].unsqueeze(1).to_broadcast([PARTS, TILES, D]),
                                    ALU.add).then_inc(resid_ready, 1)

        @block.tensor
        def _(pe):
            def keep_warm(ps, n):
                for _ in range(n):
                    nc.tensor.matmul(ps[:], idle[:, 0:PARTS], idle[:], start=True, stop=True)

            pe.wait_ge(idle_ready, 1)
            keep_warm(misc_ps, WARM_START)
            pe.wait_ge(q_loaded, 16)
            nc.tensor.matmul(row_ps[:, 0, :], wq_t, x_t, start=True, stop=True).then_inc(q_projected, 1)
            pe.wait_ge(msg_ready, 1)
            nc.tensor.matmul(row_ps[:, 1, :], wk_t, msg_t[:], start=True, stop=True).then_inc(k_projected, 1)
            pe.wait_ge(v_loaded, 16)
            pe.wait_ge(bv_loaded, 16)
            pe.wait_ge(ones_row_ready, 1)
            for c in range(CHUNKS):
                nc.tensor.matmul(mix_ps[:, c * D:(c + 1) * D], msg_t[:, c * PARTS:(c + 1) * PARTS], wv_t,
                                 start=True, stop=False)
                last = nc.tensor.matmul(mix_ps[:, c * D:(c + 1) * D], ones_row[:], bv_row[:], start=False, stop=True)
            last.then_inc(v_projected, 1)
            keep_warm(misc_ps, WARM_PROJECTED)

            def row_tile(i):
                h, t = divmod(i, TILES)
                if h % GROUP == 0 and t == 0:
                    pe.wait_ge(stacked[h // GROUP], 16 * 4)
                    pe.wait_ge(stacked_by_pool[h // GROUP], 16 * 2)
                if i == 0:
                    pe.wait_ge(q_rest_ready, 1)
                    pe.wait_ge(k_rest_ready, 1)
                if i >= ROW_BANKS:
                    pe.wait_ge(rows_maxed, i - ROW_BANKS + 1)
                nc.tensor.matmul(row_ps[:, i % ROW_BANKS, :], queries[0:SCORE_ROWS, h, t * PARTS:(t + 1) * PARTS],
                                 keys[0:SCORE_ROWS, h, :], start=True, stop=True).then_inc(rows_scored, 1)

            def turn_max(h):
                pe.wait_ge(neg_max_ready, h + 1)
                if h == 0:
                    pe.wait_ge(identity_ready, 1)
                if h >= 1:
                    pe.wait_ge(max_rows_ready, h)
                for t in range(TILES):
                    last = nc.tensor.matmul(misc_ps[SCORE_ROWS:SHIFTED_ROWS, t * PARTS:(t + 1) * PARTS],
                                            neg_max_parts[:, h, t, :], identity_b[:], start=True, stop=True)
                last.then_inc(max_turned, 1)

            def col_tile(s):
                h, c = divmod(s, CHUNKS)
                if c == 0:
                    pe.wait_ge(max_rows_ready, h + 1)
                if s == 0:
                    pe.wait_ge(ones_ready, 1)
                    pe.wait_ge(bias_cols_ready, 1)
                if s >= COL_BANKS:
                    pe.wait_ge(exps_done, s - COL_BANKS + 1)
                ps = col_ps[:, s % COL_BANKS, :]
                masked_later = s in POOL_TILES or s in DVE_TILES
                last = nc.tensor.matmul(ps, keys[0:SHIFTED_ROWS, h, c * PARTS:(c + 1) * PARTS],
                                        queries[0:SHIFTED_ROWS, h, :], start=True, stop=masked_later)
                if not masked_later:
                    last = nc.tensor.matmul(ps, identity_b[:], bias_cols[:, c, :], start=False, stop=True)
                last.then_inc(cols_scored, 1)

            def mix(g, c):
                tiles = [CHUNKS * (GROUP * g + j) + c for j in range(GROUP)]
                pe.wait_ge(exps_done, tiles[-1] + 1)
                first, end = c == 0, c == CHUNKS - 1
                for masker_tiles, kept in ((POOL_TILES, edges_kept_by_pool), (DVE_TILES, edges_kept_by_dve)):
                    masked_here = [n for n, s in enumerate(masker_tiles) if s in tiles]
                    if masked_here:
                        pe.wait_ge(kept, masked_here[-1] + 1)
                if first and g == 0:
                    pe.wait_ge(values_ready, 1)
                if first and g > 0:
                    pe.wait_ge(rows_maxed, N_HEADS * TILES)
                pieces = len(mixed_ps[g])
                for piece in range(pieces):
                    cols = slice(piece * T // pieces, (piece + 1) * T // pieces)
                    for j in range(GROUP):
                        h = GROUP * g + j
                        last = nc.tensor.matmul(mixed_ps[g][piece][j * LANE:(j + 1) * LANE, :], values[:, c, h, :],
                                                probs[:, h, c, cols], start=first, stop=end)
                    if end:
                        last.then_inc(mixed_done, 1)

            def turn_mixed(ps, g, tiles):
                for n, t in enumerate(tiles):
                    last = nc.tensor.transpose(ps[:, n * PARTS:(n + 1) * PARTS],
                                               mixed[:, g, t * PARTS:(t + 1) * PARTS], identity)
                last.then_inc(mixed_turned, 1)

            def start_y(t):
                nc.tensor.matmul(y_ps[t], identity, resid[:, t, :], start=True, stop=False)

            def turn_attended(half):
                pe.wait_ge(attended_ready, 2 + half)
                for n in range(2):
                    t = 2 * half + n
                    last = nc.tensor.transpose(turned_ps[half][:, n * PARTS:(n + 1) * PARTS],
                                               attended[:, t, :, :].rearrange("p h d -> p (h d)"), identity)
                last.then_inc(attended_turned, 1)

            def project_out(half):
                pe.wait_ge(attended_t_ready, half + 1)
                for t in (2 * half, 2 * half + 1):
                    nc.tensor.matmul(y_ps[t], attended_t[:, t * PARTS:(t + 1) * PARTS], wo_t,
                                     start=False, stop=True).then_inc(projected_out, 1)

            n_tiles = N_HEADS * TILES
            for i in range(LEAD - 1):
                row_tile(i)
                if i == TURN_FIRST_AT:
                    turn_max(0)
                if i == 0:
                    pe.wait_ge(values_ready, 1)
                keep_warm(mix_ps, WARM_RAMP)
            for s in range(n_tiles):
                if s + LEAD - 1 < n_tiles:
                    row_tile(s + LEAD - 1)
                if s % CHUNKS == CHUNKS - 1 and s + 1 < n_tiles:
                    turn_max((s + 1) // CHUNKS)
                col_tile(s)
                for c, after in enumerate(MIX_AFTER):
                    if s == after:
                        mix(0, c)
            pe.wait_ge(mixed_copied, 1)
            turn_mixed(mix_ps[:], 0, range(TILES))
            for c in range(CHUNKS):
                mix(1, c)
            pe.wait_ge(exps_done, n_tiles)
            pe.wait_ge(rows_maxed, N_HEADS * TILES)
            for half in range(2):
                pe.wait_ge(mixed_copied, 2 + half)
                turn_mixed(col_ps[:, half, :], 1, (2 * half, 2 * half + 1))
            pe.wait_ge(max_rows_ready, N_HEADS)
            pe.wait_ge(resid_ready, 1)
            start_y(0)
            turn_attended(0)
            start_y(1)
            start_y(2)
            turn_attended(1)
            project_out(0)
            start_y(3)
            project_out(1)

        @block.scalar
        def _(act):
            nc.scalar.preload_act_table(ACT.Exp)
            act.wait_ge(q_loaded, 16)
            act.wait_ge(q_projected, 1)
            nc.scalar.activation(parts[:, 0, :], row_ps[:, 0, :], ACT.Identity,
                                 bias=bq_col).then_inc(q_first_part_ready, 1)
            act.wait_ge(k_loaded, 16)
            act.wait_ge(k_projected, 1)
            nc.scalar.activation(parts[:, 3, :], row_ps[:, 1, :], ACT.Identity,
                                 bias=bk_col).then_inc(k_first_part_ready, 1)

            act.wait_ge(v_projected, 1)
            nc.scalar.copy(values[:, :, :, 0:D_HEAD],
                           mix_ps[:].rearrange("p (c h d) -> p c h d", c=CHUNKS, h=N_HEADS)).then_inc(values_ready, 1)
            act.wait_ge(bias_cols_ready, 1)
            nc.scalar.activation(edges_cols[:], bias_cols[:], ACT.Identity, bias=1.0,
                                 scale=-1.0 / MASK_BIAS).then_inc(edges_cols_ready, 1)

            def max_rows(h):
                act.wait_ge(max_turned, h + 1)
                nc.scalar.copy(queries[SCORE_ROWS:SHIFTED_ROWS, h, :],
                               misc_ps[SCORE_ROWS:SHIFTED_ROWS, :]).then_inc(max_rows_ready, 1)

            max_rows(0)
            for s in range(N_HEADS * CHUNKS):
                h, c = divmod(s, CHUNKS)
                act.wait_ge(cols_scored, s + 1)
                nc.scalar.activation(probs[:, h, c, :], col_ps[:, s % COL_BANKS, :], ACT.Exp,
                                     scale=SCORE_SCALE).then_inc(exps_done, 1)
                if c == MAX_ROWS_AFTER and h + 1 < N_HEADS:
                    max_rows(h + 1)
                if s == COPY_AFTER:
                    act.wait_ge(mixed_done, 1)
                    nc.scalar.copy(mixed[:, 0, :], mix_ps[:]).then_inc(mixed_copied, 1)
            nc.scalar.preload_act_table(ACT.Sqrt)
            for half in range(2):
                act.wait_ge(mixed_done, 2 + half)
                cols = slice(half * T // 2, (half + 1) * T // 2)
                nc.scalar.copy(mixed[:, 1, cols], mixed_ps[1][half]).then_inc(mixed_copied, 1)
            for half in range(2):
                act.wait_ge(attended_turned, half + 1)
                nc.scalar.copy(attended_t[:, half * T // 2:(half + 1) * T // 2],
                               turned_ps[half][:, 0:T // 2]).then_inc(attended_t_ready, 1)

            def take_root(half):
                act.wait_ge(moments_ready, 2 * (half + 1))
                nc.scalar.activation(deviation[:, 2 * half:2 * half + 2], moments[:, 2 * half:2 * half + 2, 1],
                                     ACT.Sqrt, bias=EPS).then_inc(deviation_ready, 1)

            take_root(0)
            act.wait_ge(minus_mean_ready, 1)
            for t in range(2):
                if t == 1:
                    take_root(1)
                nc.scalar.activation(normed[:, t, :], y_ps[t], ACT.Identity, bias=minus_mean[:, t:t + 1],
                                     scale=rstd[:, t:t + 1]).then_inc(normed_by_act, 1)

        @block.vector
        def _(dve):
            nc.vector.memset(idle[:], 0.0).then_inc(idle_ready, 1)
            nc.vector.memset(ones_row[:], 1.0).then_inc(ones_row_ready, 1)
            dve.wait_ge(k_loaded, 16)
            nc.vector.tensor_scalar(msg_t[:], h_t, edge_col, None, ALU.add).then_inc(msg_ready, 1)
            dve.wait_ge(q_loaded, 16)
            dve.wait_ge(q_first_part_ready, 1)
            nc.vector.scalar_tensor_tensor(parts[:, 1, :], row_ps[:, 0, :], bq_col, parts[:, 0, :],
                                           ALU.add, ALU.subtract).then_inc(q_middle_part_ready, 1)
            nc.vector.scalar_tensor_tensor(q_rest[:], row_ps[:, 0, :], bq_col, parts[:, 0, :],
                                           ALU.add, ALU.subtract).then_inc(q_rest_ready, 1)
            dve.wait_ge(k_first_part_ready, 1)
            nc.vector.scalar_tensor_tensor(parts[:, 4, :], row_ps[:, 1, :], bk_col, parts[:, 3, :],
                                           ALU.add, ALU.subtract).then_inc(k_middle_part_ready, 1)
            nc.vector.scalar_tensor_tensor(k_rest[:], row_ps[:, 1, :], bk_col, parts[:, 3, :],
                                           ALU.add, ALU.subtract).then_inc(k_rest_ready, 1)
            dve.wait_ge(q_middle_part_ready, 1)
            dve.wait_ge(q_rest_ready, 1)
            nc.vector.tensor_tensor(parts[:, 2, :], q_rest[:], parts[:, 1, :],
                                    ALU.subtract).then_inc(q_last_part_ready, 1)
            dve.wait_ge(k_middle_part_ready, 1)
            dve.wait_ge(k_rest_ready, 1)
            nc.vector.tensor_tensor(parts[:, 5, :], k_rest[:], parts[:, 4, :],
                                    ALU.subtract).then_inc(k_last_part_ready, 1)
            dve.wait_ge(adj_rows_loaded, 16)
            nc.vector.tensor_scalar(bias_rows[:], adj_rows[:], 0, MASK_BIAS, ALU.is_equal,
                                    ALU.mult).then_inc(bias_rows_ready, 1)
            dve.wait_ge(adj_cols_loaded, 16)
            nc.vector.tensor_scalar(bias_cols[:], adj_cols[:], 0, MASK_BIAS, ALU.is_equal,
                                    ALU.mult).then_inc(bias_cols_ready, 1)
            dve.wait_ge(bias_rows_ready, 1)

            def normalise(n, ps, g, tiles):
                heads = slice(GROUP * g, GROUP * (g + 1))
                t = slice(tiles[0], tiles[-1] + 1)
                ps = ps.rearrange("p (t h d) -> p t h d", t=len(tiles), h=GROUP)
                dve.wait_ge(mixed_turned, n + 1)
                nc.vector.tensor_scalar(total[:, t, heads], ps[:, :, :, D_HEAD], TINY, None,
                                        ALU.max).then_inc(total_ready, 1)
                dve.wait_ge(total_ready, n + 1)
                nc.vector.reciprocal(per_total[:, t, heads], total[:, t, heads]).then_inc(per_total_ready, 1)
                dve.wait_ge(per_total_ready, n + 1)
                nc.vector.tensor_tensor(attended[:, t, heads, :], ps[:, :, :, 0:D_HEAD],
                                        per_total[:, t, heads].unsqueeze(3)
                                        .to_broadcast([PARTS, len(tiles), GROUP, D_HEAD]),
                                        ALU.mult).then_inc(attended_ready, 1)

            def cut_max(h):
                dve.wait_ge(rows_maxed, TILES * (h + 1))
                nc.vector.tensor_tensor(neg_max_parts[:, h, :, 1], neg_max[:, h, :, 0], neg_max_parts[:, h, :, 0],
                                        ALU.subtract).then_inc(neg_max_ready, 1)

            for i in range(N_HEADS * TILES):
                h, t = divmod(i, TILES)
                dve.wait_ge(rows_scored, i + 1)
                if i >= MASKED_SLOTS:
                    dve.wait_ge(rows_maxed, i - MASKED_SLOTS + 1)
                nc.vector.tensor_tensor_reduce(out=masked[:, i % MASKED_SLOTS, :],
                                               in0=row_ps[:, i % ROW_BANKS, :], in1=bias_rows[:, t, :],
                                               scale=-1.0, scalar=NEG_MAX_CEILING, op0=ALU.add, op1=ALU.min,
                                               accum_out=neg_max[:, h, t, 0:1]).then_inc(rows_maxed, 1)
                if t == TILES - 1:
                    cut_max(h)
            for s in DVE_TILES:
                h, c = divmod(s, CHUNKS)
                dve.wait_ge(exps_done, s + 1)
                nc.vector.scalar_tensor_tensor(probs[:, h, c, :], probs[:, h, c, :], LARGEST, edges_cols[:, c, :],
                                               ALU.min, ALU.mult).then_inc(edges_kept_by_dve, 1)
            normalise(0, mix_ps[:], 0, range(TILES))
            for half in range(2):
                normalise(1 + half, col_ps[:, half, 0:T // 2], 1, (2 * half, 2 * half + 1))

            def stats_of(half):
                for t in (2 * half, 2 * half + 1):
                    dve.wait_ge(projected_out, t + 1)
                    nc.vector.bn_stats(stats[:, t, :], y_ps[t]).then_inc(stats_ready, 1)

            def moments_of(half):
                for t in (2 * half, 2 * half + 1):
                    dve.wait_ge(stats_ready, t + 1)
                    nc.vector.bn_aggr(moments[:, t, :], stats[:, t, :]).then_inc(moments_ready, 1)

            def per_deviation(half):
                tiles = slice(2 * half, 2 * half + 2)
                dve.wait_ge(deviation_ready, half + 1)
                nc.vector.reciprocal(rstd[:, tiles], deviation[:, tiles]).then_inc(rstd_ready, 1)
                dve.wait_ge(rstd_ready, half + 1)

            stats_of(0)
            moments_of(0)
            stats_of(1)
            per_deviation(0)
            nc.vector.scalar_tensor_tensor(minus_mean[:], moments[:, 0:2, 0], -1.0, rstd[:, 0:2],
                                           ALU.mult, ALU.mult).then_inc(minus_mean_ready, 1)
            moments_of(1)
            per_deviation(1)
            for t in (2, 3):
                nc.vector.tensor_scalar(normed[:, t, :], y_ps[t], moments[:, t, 0:1], rstd[:, t:t + 1],
                                        ALU.subtract, ALU.mult).then_inc(normed_ready, 1)


def kernel(x, adj, L0_gnn_h_neigh, L0_gnn_Wq, L0_gnn_bq, L0_gnn_Wk, L0_gnn_bk, L0_gnn_Wv, L0_gnn_bv,
           L0_gnn_Wo, L0_gnn_bo, L0_gnn_E):
    import numpy as np
    import concourse.bacc as bacc
    from concourse.bass_utils import run_bass_kernel_spmd

    def dim_major(a):
        return a.reshape(len(a), N_GROUPS, GROUP, D_HEAD).transpose(0, 1, 3, 2).reshape(len(a), D_MODEL)

    x, adj = np.asarray(x), np.asarray(adj)
    arrays = {
        "q_pack": np.concatenate([x.T, dim_major(np.asarray(L0_gnn_Wq).T), dim_major(np.asarray(L0_gnn_bq)[None, :]).T], 1),
        "k_pack": np.concatenate([np.asarray(L0_gnn_h_neigh).T, dim_major(np.asarray(L0_gnn_Wk).T),
                                  dim_major(np.asarray(L0_gnn_bk)[None, :]).T, np.asarray(L0_gnn_E).T], 1),
        "v_pack": np.concatenate([np.asarray(L0_gnn_Wv).T, np.asarray(L0_gnn_Wo).T,
                                  np.eye(PARTS, dtype=np.float32)], 1),
        "x": x,
        "adj": adj,
        "adj_t": adj.T,
        "bv": np.asarray(L0_gnn_bv)[None, :],
        "bo": np.asarray(L0_gnn_bo)[None, :],
    }
    arrays = {name: np.ascontiguousarray(a) for name, a in arrays.items()}
    nc = bacc.Bacc("TRN2", target_bir_lowering=False, num_devices=1)
    args = [nc.dram_tensor(name, a.shape, mybir.dt.from_np(a.dtype), kind="ExternalInput").ap()
            for name, a in arrays.items()]
    out = nc.dram_tensor("out", (N_TARGETS, D_MODEL), mybir.dt.float32, kind="ExternalOutput").ap()
    graph_attention(nc, *args, out)
    result = run_bass_kernel_spmd(nc, [arrays], core_ids=[0])
    return result.results[0]["out"]
```
